# Optimizing a Trainium2 kernel written in Bass

```python
import numpy as np
import jax
import jax.numpy as jnp

def _softmax(x, axis=-1):
    return jax.nn.softmax(x, axis=axis)

def _gelu(x):
    return jax.nn.gelu(x, approximate=True)

def _silu(x):
    return jax.nn.silu(x)

def _sigmoid(x):
    return jax.nn.sigmoid(x)

def _layernorm(x, axis=-1, eps=1e-05):
    m = jnp.mean(x, axis=axis, keepdims=True)
    v = jnp.var(x, axis=axis, keepdims=True)
    return (x - m) / jnp.sqrt(v + eps)

def _scatter_add(tgt, idx, src, axis=0):
    return tgt.at[idx].add(src)

def _segment_sum(src, seg, n):
    return jax.ops.segment_sum(src, seg, n)
kernel_name = 'mk_seq_postln_d1_jaxref_r8_5bcde5'

def setup_inputs(seed: int=0):
    np.random.seed(seed)
    _w = jnp.asarray

    def _L0_attn_setup():
        import jax, jax.numpy as jnp
        import numpy as np
        HEADS = 64
        DIM_HEAD = 64
        SCALE = DIM_HEAD ** (-0.5)
        EPS = 1e-06
        key = jax.random.key(seed)
        ks = jax.random.split(key, 6)
        b, s, dim = (2, 512, 128)
        inner = HEADS * DIM_HEAD
        std = 0.02
        return {'x': jax.random.normal(ks[0], (b, s, dim), dtype=jnp.float32), 'Wq': jax.random.normal(ks[1], (dim, inner), dtype=jnp.float32) * std, 'Wk': jax.random.normal(ks[2], (dim, inner), dtype=jnp.float32) * std, 'Wv': jax.random.normal(ks[3], (dim, inner), dtype=jnp.float32) * std, 'Wo': jax.random.normal(ks[4], (inner, dim), dtype=jnp.float32) * std, 'bo': jnp.zeros((dim,), dtype=jnp.float32)}
    _L0_attn_in = _L0_attn_setup()

    def _L0_ffn_setup():
        import jax, jax.numpy as jnp
        import numpy as np
        BLOCK = 16
        _GRID = jnp.array([0.0, 0.5, 1.0, 1.5, 2.0, 3.0, 4.0, 6.0], dtype=jnp.float32)
        _MID = jnp.array([0.25, 0.75, 1.25, 1.75, 2.5, 3.5, 5.0], dtype=jnp.float32)

        def fp4_quant_dequant(x):
            shape = x.shape
            xb = x.reshape(shape[:-1] + (shape[-1] // BLOCK, BLOCK))
            scale = jnp.max(jnp.abs(xb), axis=-1, keepdims=True) / 6.0
            scale = jnp.maximum(scale, jnp.float32(1e-12))
            xn = xb / scale
            idx = jnp.searchsorted(_MID, jnp.abs(xn))
            q = _GRID[idx] * jnp.sign(xn) * scale
            return q.reshape(shape)

        def fp4_linear(x, w):
            xq = fp4_quant_dequant(x)
            wq = fp4_quant_dequant(w)
            return jnp.einsum('bsk,nk->bsn', xq, wq)
        key = jax.random.key(seed)
        k1, k2, k3, k4 = jax.random.split(key, 4)
        H, I = (128, 352)
        x = jax.random.normal(k1, (4, 512, H), dtype=jnp.float32)
        w_gate = jax.random.normal(k2, (I, H), dtype=jnp.float32) * 0.02
        w_up = jax.random.normal(k3, (I, H), dtype=jnp.float32) * 0.02
        w_down = jax.random.normal(k4, (H, I), dtype=jnp.float32) * 0.02
        return {'x': x, 'w_gate': w_gate, 'w_up': w_up, 'w_down': w_down}
    _L0_ffn_in = _L0_ffn_setup()
    _d = {'L0_attn_x': _L0_attn_in['x'], 'L0_attn_Wq': _L0_attn_in['Wq'], 'L0_attn_Wk': _L0_attn_in['Wk'], 'L0_attn_Wv': _L0_attn_in['Wv'], 'L0_attn_Wo': _L0_attn_in['Wo'], 'L0_attn_bo': _L0_attn_in['bo'], 'L0_ffn_w_gate': _L0_ffn_in['w_gate'], 'L0_ffn_w_up': _L0_ffn_in['w_up'], 'L0_ffn_w_down': _L0_ffn_in['w_down']}
    _x0 = _d['L0_attn_x']
    _d['L0_attn_x'] = jax.random.normal(jax.random.fold_in(jax.random.key(seed), 1), (32, 256, 128), dtype=_x0.dtype)
    del _x0
    return _d

def reference(L0_attn_x, L0_attn_Wq, L0_attn_Wk, L0_attn_Wv, L0_attn_Wo, L0_attn_bo, L0_ffn_w_gate, L0_ffn_w_up, L0_ffn_w_down):

    def _L0_attn_ref(x, Wq, Wk, Wv, Wo, bo):
        import jax, jax.numpy as jnp
        import numpy as np
        HEADS = 64
        DIM_HEAD = 64
        SCALE = DIM_HEAD ** (-0.5)
        EPS = 1e-06
        b, s, dim = x.shape
        h, dh = (HEADS, DIM_HEAD)
        q = (x @ Wq).reshape(b, s, h, dh)
        k = (x @ Wk).reshape(b, s, h, dh)
        v = (x @ Wv).reshape(b, s, h, dh)
        q = jax.nn.relu(q) * SCALE
        k = jax.nn.relu(k)
        kv = jnp.einsum('bsid,bsjd->bsdj', k, v)
        out = jnp.einsum('bsid,bsdj->bsij', q, kv)
        q_norm = jnp.einsum('bsid,bsd->bsi', q, k.sum(axis=2))
        out = out / (q_norm[..., None] + EPS)
        out = out.reshape(b, s, h * h)
        return out @ Wo + bo

    def _L0_ffn_ref(x, w_gate, w_up, w_down):
        import jax, jax.numpy as jnp
        import numpy as np
        BLOCK = 16
        _GRID = jnp.array([0.0, 0.5, 1.0, 1.5, 2.0, 3.0, 4.0, 6.0], dtype=jnp.float32)
        _MID = jnp.array([0.25, 0.75, 1.25, 1.75, 2.5, 3.5, 5.0], dtype=jnp.float32)

        def fp4_quant_dequant(x):
            shape = x.shape
            xb = x.reshape(shape[:-1] + (shape[-1] // BLOCK, BLOCK))
            scale = jnp.max(jnp.abs(xb), axis=-1, keepdims=True) / 6.0
            scale = jnp.maximum(scale, jnp.float32(1e-12))
            xn = xb / scale
            idx = jnp.searchsorted(_MID, jnp.abs(xn))
            q = _GRID[idx] * jnp.sign(xn) * scale
            return q.reshape(shape)

        def fp4_linear(x, w):
            xq = fp4_quant_dequant(x)
            wq = fp4_quant_dequant(w)
            return jnp.einsum('bsk,nk->bsn', xq, wq)
        gate = fp4_linear(x, w_gate)
        y = fp4_linear(x, w_up)
        h = jax.nn.silu(gate) * y
        return fp4_linear(h, w_down)
    x = L0_attn_x
    x = _layernorm(x + _L0_attn_ref(x, L0_attn_Wq, L0_attn_Wk, L0_attn_Wv, L0_attn_Wo, L0_attn_bo), axis=-1)
    x = _layernorm(x + _L0_ffn_ref(x, L0_ffn_w_gate, L0_ffn_w_up, L0_ffn_w_down), axis=-1)
    return x

_drawn_inputs = setup_inputs


def setup_inputs(seed=0):
    import zlib

    import numpy as np

    out = dict(_drawn_inputs(seed))
    spreads = {'L0_attn_bo': (0.0, 0.1)}
    factors = {'L0_attn_Wk': 5.071, 'L0_ffn_w_gate': 5.777, 'L0_ffn_w_up': 5.683, 'L0_ffn_w_down': 5.703}
    for name, (base, spread) in spreads.items():
        noise = np.random.default_rng([zlib.crc32(name.encode()), seed]).standard_normal(out[name].shape)
        drawn = base * np.exp(spread * noise) if base else spread * noise
        out[name] = jnp.asarray(drawn.astype(out[name].dtype))
    for name, factor in factors.items():
        out[name] = (out[name] * factor).astype(out[name].dtype)
    return out
```

```python
from contextlib import ExitStack

import concourse.bass as bass
from concourse import mybir

F32 = mybir.dt.float32
BF16 = mybir.dt.bfloat16
ALU = mybir.AluOpType
ACT = mybir.ActivationFunctionType
AX = mybir.AxisListType

P = 128
DIM = 128
HEADS = 64
DH = 64
HALF = DH // 2
T = 128
S = T // 2
VW = HALF + 1
PW = 2 * VW
FFN = 352
BLK = 16
EPS_NORM = 1e-6
EPS_LN = 1e-5
SCALE = DH ** -0.5

EC = 8
NC = HALF // EC
G = 8
NG = S // G
SLOTS = 3
QR = 4
OR = 4
MIDS = [0.25, 0.75, 1.25, 1.75, 2.5, 3.5, 5.0]
WP = 88
DOWN = [(0, 128), (128, 128), (256, 96)]

USES = ([("k", c) for c in range(NC)] + [("out", g) for g in range(NG)]
        + [("v", c) for c in range(NC)] + [("q", c) for c in range(NC)])
SLOT = {u: i % SLOTS for i, u in enumerate(USES)}


def attention_ffn(nc, x, wq, wk, wv, wo, bo, w_gate, w_up, w_down, out):
    NT = x.shape[0] * x.shape[1] // T
    x_t = x.rearrange("b s c -> (b s) c")
    out_t = out.rearrange("b s c -> (b s) c")

    ctx = ExitStack()
    with ctx:
        def sb(name, shape, dt=F32):
            return ctx.enter_context(nc.sbuf_tensor(name, shape, dt))

        def sem(name):
            return ctx.enter_context(nc.semaphore(name))

        w_kvq = {k: sb(f"w_{k}", [P, 2, HALF * P], BF16) for k in "kvq"}
        w_o = sb("w_o", [P, 2, HALF * DIM], BF16)
        w_gu = sb("w_gu", [P, 2 * FFN])
        w_dn = sb("w_dn", [P, 3, DIM])
        k_acc = sb("k_acc", [P, EC * T])
        ks = sb("ks", [P, T])
        q32 = sb("q32", [P, QR, EC * T])
        q_nat = sb("q_nat", [P, 2 * 2 * HALF * S], BF16)
        q_bd = sb("q_bd", [P, 2 * 2 * DH * S], BF16)
        v_st = sb("v_st", [P, 2 * 2 * S * VW], BF16)
        o_st = sb("o_st", [P, 2 * 2 * S * HALF], BF16)
        swap = sb("swap", [P, 2 * S * VW], BF16)
        o32 = sb("o32", [P, OR, G * DH])
        nrm = sb("nrm", [P, 2, G])
        rec = sb("rec", [P, 2, G])
        xT = sb("xT", [P, 2, T], BF16)
        x_in = sb("x_in", [T, DIM])
        x_res = sb("x_res", [T, DIM])
        bo_b = sb("bo_b", [P, DIM])
        ident = sb("ident", [P, P])
        both = sb("both", [P, P])
        consts = sb("consts", [P, 2])
        r1, x1, xa, xsgn, xc, xq = (sb(v, [T, DIM]) for v in ("r1", "x1", "xa", "xsgn", "xc", "xq"))
        xqT = sb("xqT", [P, T])
        xsc = sb("xsc", [T, 2, DIM // BLK])
        sig, h, ha, hc, hq, hss = (sb(v, [T, FFN]) for v in ("sig", "h", "ha", "hc", "hq", "hss"))
        hsgn = sb("hsgn", [T, FFN], BF16)
        hsc = sb("hsc", [T, 2, FFN // BLK])
        hqT = sb("hqT", [P, 3, T])
        x1b, r2, y_out = (sb(v, [T, DIM]) for v in ("x1b", "r2", "y_out"))
        st1, st2 = sb("st1", [T, 6]), sb("st2", [T, 6])
        mv1, mv2 = sb("mv1", [T, 2]), sb("mv2", [T, 2])
        ve1, rs1, ve2, rs2 = (sb(v, [T, 1]) for v in ("ve1", "rs1", "ve2", "rs2"))

        ps = ctx.enter_context(nc.psum_tensor("ps", [P, 8, 512], F32))
        TB0, TB1 = ps[:, 2 * SLOTS, :], ps[:, 2 * SLOTS + 1, :]

        def slot_cols(u):
            k = 2 * SLOT[u]
            return ps[:, k:k + 2, :].rearrange("p b (e t) -> p (b e) t", t=P)

        qbd = q_bd[:, :].rearrange("p (l c m s) -> p l c m s", l=2, c=2, s=S)
        qmat = q_bd[:, :].rearrange("p (l m s) -> p l m s", l=2, s=S)
        qnat = q_nat[:, :].rearrange("p (l a e s) -> p l a e s", l=2, a=2, s=S)
        vst = v_st[:, :].rearrange("p (l b s e) -> p l b s e", l=2, b=2, s=S)
        ost = o_st[:, :].rearrange("p (l b s e) -> p l b s e", l=2, b=2, s=S)
        omat = o_st[:, :].rearrange("p (l t e) -> p l t e", l=2, t=T)
        wmat = {k: w_kvq[k][:, :, :].rearrange("p l (e m) -> p l e m", m=P) for k in "kvq"}
        womat = w_o[:, :, :].rearrange("p l (e n) -> p l e n", n=DIM)

        stage = {"k": q_bd[:, 0:8192].bitcast(F32), "v": q_bd[:, 8192:16384].bitcast(F32),
                 "q": q32[:, :, :].rearrange("p r e -> p (r e)"), "o": q_nat[:, :].bitcast(F32)}
        gu_raw, gu_abs, gu_q, gu_m = (v_st[:, i * 2048:(i + 1) * 2048].bitcast(F32) for i in range(4))
        dn_raw, dn_abs, dn_q, dn_m = (o_st[:, i * 704:(i + 1) * 704].bitcast(F32) for i in range(4))
        w_sc = o_st[:, 2816:3072].bitcast(F32)
        split_src = {k: stage[k].rearrange("p (h i d) -> p i h d", h=2, i=HALF) for k in "kvq"}

        s_wload = {k: sem(f"s_wload_{k}") for k in "kvqo"}
        s_fload, s_whi, s_wlo, s_const, s_wstep, s_wquant, s_wT, s_ffnw, s_iota = (
            sem(f"s_{v}") for v in "fload whi wlo const wstep wquant wT ffnw iota".split())
        s_x = sem("s_x")
        s_xps = sem("s_xps")
        s_xhi, s_xlo = sem("s_xhi"), sem("s_xlo")
        s_done = {k: sem(f"s_done_{k}") for k in ("k", "v", "q", "out")}
        s_read = {k: sem(f"s_read_{k}") for k in ("k", "v", "q", "out")}
        s_kfirst = sem("s_kfirst")
        s_tree = sem("s_tree")
        s_ksps, s_ks = sem("s_ksps"), sem("s_ks")
        s_vhi, s_qhi, s_qlo = sem("s_vhi"), sem("s_qhi"), sem("s_qlo")
        s_vswap, s_qbd = sem("s_vswap"), sem("s_qbd")
        s_nrm, s_rec = sem("s_nrm"), sem("s_rec")
        s_ohi, s_olo, s_oswap = sem("s_ohi"), sem("s_olo"), sem("s_oswap")
        (s_xres, s_xb, s_y, s_r1, s_st1, s_agg1, s_ve1, s_rs1, s_x1, s_xabs, s_xmax, s_xsc, s_xrs, s_xa, s_xc, s_xs,
         s_xsgn, s_xss, s_xq, s_xqps, s_xqT, s_gate, s_up, s_sig, s_gs, s_h) = (sem(f"s_{v}") for v in (
             "xres xb y r1 st1 agg1 ve1 rs1 x1 xabs xmax xsc xrs xa xc xs xsgn xss xq xqps xqT gate up sig gs h").split())
        (s_habs, s_hmax, s_hsc, s_hrs, s_ha, s_hc, s_hs, s_hsgn, s_hss, s_hq, s_hps, s_hqT, s_dn, s_x1b, s_r2, s_st2, s_agg2,
         s_ve2, s_rs2, s_yo, s_store) = (sem(f"s_{v}") for v in (
             "habs hmax hsc hrs ha hc hs hsgn hss hq hps hqT dn x1b r2 st2 agg2 ve2 rs2 yo store").split())

        PER = {"k": NC - 1, "v": NC, "q": NC, "out": NG}

        def slot_read(it, u):
            kind, c = u
            if u == ("k", 0):
                return s_kfirst, it + 1
            return s_read[kind], (it - 1 if kind == "out" else it) * PER[kind] + (c if kind == "k" else c + 1)

        def wait_slot(pe, it, u):
            i = USES.index(u)
            for back in range(1, 3 * len(USES)):
                j = i - back
                w, wit = USES[j % len(USES)], it + j // len(USES)
                if SLOT[w] != SLOT[u]:
                    continue
                if isinstance(it, int):
                    tile_of = wit - (w[0] == "out")
                    if wit < 0:
                        return
                    if not 0 <= tile_of < NT:
                        continue
                pe.wait_ge(*slot_read(wit, w))
                return

        def run_tiles(eng, iteration):
            for n in range(3):
                iteration(n)
            with eng.Fori(3, NT - 1) as n:
                iteration(n)
            for n in range(NT - 1, NT + 3):
                iteration(n)

        def parts(n):
            if not isinstance(n, int):
                return True, True, True, True, True
            return n < NT, n + 1 < NT, 0 <= n - 1 < NT, 0 <= n - 2 < NT, 0 <= n - 3 < NT

        block = ctx.enter_context(nc.Block())

        @block.sync
        def _(sp):
            for k, w in (("k", wk), ("v", wv), ("q", wq)):
                sp.dma_start(stage[k], w).then_inc(s_wload[k], 16)
            gu = gu_raw.rearrange("p (g q k) -> p g q k", g=2, k=DIM)
            for g, w in enumerate((w_gate, w_up)):
                sp.dma_start(gu[0:WP, g], w.rearrange("(q p) k -> p q k", p=WP)).then_inc(s_fload, 16)
            sp.dma_start(dn_raw, w_down).then_inc(s_fload, 16)
            sp.dma_start(x_in[:, :], x_t[0:T, :]).then_inc(s_x, 16)
            for j in range(2):
                sp.dma_start(stage["o"][j * HEADS:(j + 1) * HEADS, :],
                             wo.rearrange("(i j e) n -> j i (e n)", j=2, e=HALF)[j]).then_inc(s_wload["o"], 16)
            sp.dma_start(bo_b[:, :], bo.partition_broadcast(P)).then_inc(s_store, 16)

            osw = swap[0:64, 0:2 * S * HALF].rearrange("p (l e) -> p l e", l=2)
            vsw = swap[64:128, :].rearrange("p (l e) -> p l e", l=2)
            o4 = o_st[:, :].rearrange("p (l b e) -> p l b e", l=2, b=2)
            v4 = v_st[:, :].rearrange("p (l b e) -> p l b e", l=2, b=2)

            def iteration(n):
                front, more, attend, mid, back = parts(n)
                if more:
                    sp.wait_ge(s_xps, n + 1)
                    sp.dma_start(x_in[:, :], x_t[bass.ts(n + 1, T), :]).then_inc(s_x, 16)
                if mid:
                    m = n - 2
                    if back:
                        sp.wait_ge(s_r1, m)
                    sp.dma_start(x_res[:, :], x_t[bass.ts(m, T), :]).then_inc(s_xres, 16)
                if attend:
                    o = n - 1
                    sp.wait_ge(s_ohi, (o + 1) * NG)
                    sp.wait_ge(s_olo, (o + 1) * NG)
                    sp.dma_start(osw, o4[64:128, :, 0]).then_inc(s_oswap, 16)
                    sp.wait_ge(s_oswap, o * 48 + 16)
                    sp.dma_start(o4[64:128, :, 0], o4[0:64, :, 1]).then_inc(s_oswap, 16)
                if front:
                    sp.wait_ge(s_read["v"], (n + 1) * NC)
                    sp.dma_start(vsw, v4[64:128, :, 0]).then_inc(s_vswap, 16)
                if attend:
                    sp.wait_ge(s_oswap, o * 48 + 32)
                    sp.dma_start(o4[0:64, :, 1], osw).then_inc(s_oswap, 16)
                if front:
                    sp.wait_ge(s_vswap, n * 48 + 16)
                    sp.dma_start(v4[64:128, :, 0], v4[0:64, :, 1]).then_inc(s_vswap, 16)
                if back:
                    m = n - 3
                    sp.wait_ge(s_yo, m + 1)
                    sp.dma_start(out_t[bass.ts(m, T), :], y_out[:, :]).then_inc(s_store, 16)
                if front:
                    sp.wait_ge(s_vswap, n * 48 + 32)
                    sp.dma_start(v4[0:64, :, 1], vsw).then_inc(s_vswap, 16)
                    sp.wait_ge(s_qlo, (n + 1) * NC)
                    for par in range(2):
                        for ih in range(2):
                            sp.dma_start(qbd[par * 64:par * 64 + 64, :, par, ih * HALF:(ih + 1) * HALF],
                                         qnat[ih * 64:ih * 64 + 64, :, par]).then_inc(s_qbd, 16)

            run_tiles(sp, iteration)
            sp.wait_ge(s_store, 16 * (NT + 1))

        @block.tensor
        def _(pe):
            pe.wait_ge(s_const, 1)
            pe.wait_ge(s_x, 16)
            nc.tensor.transpose(TB1[:, 0:T], x_in[:, :], ident[:, :]).then_inc(s_xps, 1)
            pe.wait_ge(s_wquant, 1)
            gq = gu_q.rearrange("p (g k) -> p g k", k=DIM)
            for g in range(8):
                nc.tensor.transpose(ps[:, g // 4, (g % 4) * WP:(g % 4 + 1) * WP], gq[0:WP, g, :], ident[0:WP, 0:WP])
            pe.wait_ge(s_wquant, 2)
            for c, (k0, kn) in enumerate(DOWN):
                last = nc.tensor.transpose(ps[0:kn, 2, c * DIM:(c + 1) * DIM], dn_q[:, k0:k0 + kn], ident[:, :])
            last.then_inc(s_wT, 1)
            pe.wait_ge(s_ffnw, 2)

            def three(dst, lhs, rhs):
                nc.tensor.matmul(dst, lhs(0), rhs(0), start=True, stop=False)
                nc.tensor.matmul(dst, lhs(0), rhs(1), start=False, stop=False)
                return nc.tensor.matmul(dst, lhs(1), rhs(0), start=False, stop=True)

            def project(n, kind, c):
                wait_slot(pe, n, (kind, c))
                dst = slot_cols((kind, c))
                for e in range(EC):
                    last = three(dst[:, e, :], lambda l: wmat[kind][:, l, c * EC + e, :], lambda l: xT[:, l, :])
                last.then_inc(s_done[kind], 1)

            def out_group(n, g):
                wait_slot(pe, n, ("out", g))
                dst = slot_cols(("out", g))
                for p in range(G):
                    s = g * G + p
                    last = three(dst[:, p, 0:PW], lambda l: qmat[:, l, :, s], lambda l: vst[:, l, :, s, :])
                last.then_inc(s_done["out"], 1)

            def iteration(n):
                front, more, attend, mid, back = parts(n)
                if front:
                    pe.wait_ge(s_xhi, n + 1)
                    pe.wait_ge(s_xlo, n + 1)
                    if isinstance(n, int) and n == 0:
                        pe.wait_ge(s_wlo, 4)
                    for c in range(NC):
                        project(n, "k", c)
                if mid:
                    m = n - 2
                    pe.wait_ge(s_oswap, (m + 1) * 48)
                    if back:
                        pe.wait_ge(s_gs, m)
                    for j in range(HALF):
                        for i, (lo, lw) in enumerate(((0, 0), (0, 1), (1, 0))):
                            last = nc.tensor.matmul(TB0[:, 0:DIM], omat[:, lo, :, j], womat[:, lw, j, :],
                                                    start=(j == 0 and i == 0), stop=(j == HALF - 1 and i == 2))
                    last.then_inc(s_y, 1)
                if front:
                    pe.wait_ge(s_tree, (n + 1) * 3)
                    if back:
                        pe.wait_ge(s_h, n - 2)
                    nc.tensor.matmul(TB1[:, 0:T], both[:, :], k_acc[:, 0:T], start=True, stop=True).then_inc(s_ksps, 1)
                if attend:
                    pe.wait_ge(s_qbd, n * 64)
                    pe.wait_ge(s_vswap, n * 48)
                    for g in range(NG - 1):
                        out_group(n, g)
                if back:
                    b = n - 3
                    pe.wait_ge(s_hq, b + 1)
                    if front:
                        pe.wait_ge(s_ks, n + 1)
                    for c, (k0, kn) in enumerate(DOWN):
                        last = nc.tensor.transpose(TB1[0:kn, c * T:(c + 1) * T], hq[:, k0:k0 + kn], ident[:, :])
                    last.then_inc(s_hps, 1)
                if attend:
                    out_group(n, NG - 1)
                if front:
                    project(n, "v", 0)
                if back:
                    pe.wait_ge(s_hqT, b + 1)
                    if mid:
                        pe.wait_ge(s_r1, n - 1)
                    for c, (k0, kn) in enumerate(DOWN):
                        last = nc.tensor.matmul(TB0[:, 0:DIM], hqT[0:kn, c, :], w_dn[0:kn, c, :],
                                                start=(c == 0), stop=(c == len(DOWN) - 1))
                    last.then_inc(s_dn, 1)
                if mid:
                    pe.wait_ge(s_xq, m + 1)
                    if front and not back:
                        pe.wait_ge(s_ks, n + 1)
                    nc.tensor.transpose(TB1[:, 0:T], xq[:, :], ident[:, :]).then_inc(s_xqps, 1)
                if front:
                    for c in range(1, NC):
                        project(n, "v", c)
                    for c in range(NC):
                        project(n, "q", c)
                if more:
                    pe.wait_ge(s_x, (n + 2) * 16)
                    if mid:
                        pe.wait_ge(s_xqT, m + 1)
                    else:
                        pe.wait_ge(s_ks, n + 1)
                    nc.tensor.transpose(TB1[:, 0:T], x_in[:, :], ident[:, :]).then_inc(s_xps, 1)
                if mid:
                    pe.wait_ge(s_xqT, m + 1)
                    if back:
                        pe.wait_ge(s_r2, b + 1)
                    nc.tensor.matmul(TB0[:, 0:FFN], xqT[:, :], w_gu[:, 0:FFN], start=True, stop=True).then_inc(s_gate, 1)
                    if more:
                        pe.wait_ge(s_xlo, n + 2)
                    nc.tensor.matmul(TB1[:, 0:FFN], xqT[:, :], w_gu[:, FFN:2 * FFN],
                                     start=True, stop=True).then_inc(s_up, 1)

            run_tiles(pe, iteration)

        @block.scalar
        def _(act):
            act.wait_ge(s_xps, 1)
            nc.scalar.copy(xT[:, 0, :], TB1[:, 0:T]).then_inc(s_xhi, 1)
            for k in "kvq":
                act.wait_ge(s_wload[k], 16)
                nc.scalar.activation(wmat[k][:, 0].rearrange("p e (h m) -> p e h m", h=2), split_src[k], ACT.Copy,
                                     scale=SCALE if k == "q" else 1.0).then_inc(s_whi, 1)
            act.wait_ge(s_wload["o"], 32)
            nc.scalar.copy(w_o[:, 0, :], stage["o"]).then_inc(s_whi, 1)
            act.wait_ge(s_wT, 1)
            nc.scalar.copy(w_gu[:, :].rearrange("p (g n) -> p g n", g=2), ps[:, 0:2, 0:FFN]).then_inc(s_ffnw, 1)
            for c, (k0, kn) in enumerate(DOWN):
                last = nc.scalar.copy(w_dn[0:kn, c, :], ps[0:kn, 2, c * DIM:(c + 1) * DIM])
            last.then_inc(s_ffnw, 1)
            act.wait_ge(s_wlo, 4)

            def v_hi(n, c):
                act.wait_ge(s_done["v"], n * NC + c + 1)
                dst = vst[:, 0].rearrange("p b s e -> p e (b s)")[:, c * EC:(c + 1) * EC]
                nc.scalar.copy(dst, slot_cols(("v", c))).then_inc(s_vhi, 1)

            def q_hi(n, c):
                act.wait_ge(s_read["q"], n * NC + c + 1)
                nc.scalar.copy(qnat[:, 0, :, c * EC:(c + 1) * EC, :],
                               q32[:, c % QR, :].rearrange("p (e a s) -> p a e s", a=2, s=S)).then_inc(s_qhi, 1)

            def o_hi(o, g):
                act.wait_ge(s_read["out"], o * NG + g + 1)
                nc.scalar.copy(ost[:, 0, :, g * G:(g + 1) * G, :].rearrange("p b s e -> p s b e"),
                               o32[:, g % OR, :].rearrange("p (s b e) -> p s b e", b=2, e=HALF)).then_inc(s_ohi, 1)

            def iteration(n):
                front, more, attend, mid, back = parts(n)
                o, m, b = n - 1, n - 2, n - 3
                if back:
                    act.wait_ge(s_gate, b + 1)
                    nc.scalar.activation(sig[:, :], TB0[:, 0:FFN], ACT.Sigmoid).then_inc(s_sig, 1)
                if front:
                    act.wait_ge(s_done["k"], n * NC + 1)
                    nc.scalar.activation(k_acc[:, :].rearrange("p (e t) -> p e t", t=T), slot_cols(("k", 0)),
                                         ACT.Relu).then_inc(s_kfirst, 1)
                if back:
                    act.wait_ge(s_h, b + 1)
                    nc.scalar.activation(ha[:, :], h[:, :], ACT.Abs).then_inc(s_habs, 1)
                    nc.scalar.activation(hsgn[:, :], h[:, :], ACT.Sign).then_inc(s_hsgn, 1)
                if front:
                    act.wait_ge(s_ksps, n + 1)
                    nc.scalar.copy(ks[:, :], TB1[:, 0:T]).then_inc(s_ks, 1)
                if attend:
                    o_hi(o, 0)
                if mid:
                    act.wait_ge(s_x1, m + 1)
                    nc.scalar.activation(xa[:, :], x1[:, :], ACT.Abs).then_inc(s_xabs, 1)
                    nc.scalar.activation(xsgn[:, :], x1[:, :], ACT.Sign).then_inc(s_xsgn, 1)
                if attend:
                    for g in range(1, NG):
                        o_hi(o, g)
                if back:
                    act.wait_ge(s_hps, b + 1)
                    for c, (k0, kn) in enumerate(DOWN):
                        last = nc.scalar.copy(hqT[0:kn, c, :], TB1[0:kn, c * T:(c + 1) * T])
                    last.then_inc(s_hqT, 1)
                if front:
                    v_hi(n, 0)
                    v_hi(n, 1)
                if mid:
                    act.wait_ge(s_xqps, m + 1)
                    nc.scalar.copy(xqT[:, :], TB1[:, 0:T]).then_inc(s_xqT, 1)
                if front:
                    v_hi(n, 2)
                    v_hi(n, 3)
                    for c in range(NC):
                        q_hi(n, c)
                if more:
                    act.wait_ge(s_xps, n + 2)
                    nc.scalar.copy(xT[:, 0, :], TB1[:, 0:T]).then_inc(s_xhi, 1)

            run_tiles(act, iteration)

        def blocks(a):
            return a.rearrange("p (b k) -> p b k", k=BLK)

        def per_block(a, like):
            return a.unsqueeze(2).to_broadcast([like.shape[0], like.shape[1] // BLK, BLK])

        @block.vector
        def _(dve):
            nc.vector.memset(consts[:, 0:1], -0.5)
            nc.vector.memset(consts[:, 1:2], EPS_LN).then_inc(s_iota, 1)
            steps = [0]

            def link(ins):
                steps[0] += 1
                ins.then_inc(s_wstep, 1)
                dve.wait_ge(s_wstep, steps[0])

            for i, (np_, raw, ab, q, mask) in enumerate(((WP, gu_raw, gu_abs, gu_q, gu_m), (P, dn_raw, dn_abs, dn_q, dn_m))):
                raw, ab, q, mask = raw[0:np_], ab[0:np_], q[0:np_], mask[0:np_]
                nb = raw.shape[1] // BLK
                sc, rs = w_sc[0:np_, 0:nb], w_sc[0:np_, 64:64 + nb]
                dve.wait_ge(s_fload, 48)
                link(nc.vector.tensor_reduce(sc, blocks(raw), AX.X, ALU.max, apply_absolute_value=True))
                link(nc.vector.tensor_scalar(sc, sc, 1.0 / 6.0, 1e-12, ALU.mult, ALU.max))
                link(nc.vector.reciprocal(rs, sc))
                link(nc.vector.scalar_tensor_tensor(out=ab, in0=raw, scalar=-1.0, in1=raw, op0=ALU.mult, op1=ALU.max))
                link(nc.vector.tensor_tensor(blocks(ab), blocks(ab), per_block(rs, raw), ALU.mult))
                link(nc.vector.tensor_scalar(q, ab, MIDS[6], 2.0, ALU.is_gt, ALU.mult))
                for k in (5, 4):
                    link(nc.vector.scalar_tensor_tensor(out=q, in0=ab, scalar=MIDS[k], in1=q, op0=ALU.is_gt, op1=ALU.add))
                link(nc.vector.tensor_scalar(mask, ab, MIDS[0], None, ALU.is_gt))
                for k in (1, 2, 3):
                    link(nc.vector.scalar_tensor_tensor(out=mask, in0=ab, scalar=MIDS[k], in1=mask, op0=ALU.is_gt,
                                                        op1=ALU.add))
                link(nc.vector.scalar_tensor_tensor(out=q, in0=mask, scalar=0.5, in1=q, op0=ALU.mult, op1=ALU.add))
                link(nc.vector.tensor_scalar(mask, raw, 0.0, 2.0, ALU.is_ge, ALU.mult))
                link(nc.vector.scalar_tensor_tensor(out=q, in0=mask, scalar=-1.0, in1=q, op0=ALU.add, op1=ALU.mult))
                nc.vector.tensor_tensor(blocks(q), blocks(q), per_block(sc, raw), ALU.mult).then_inc(s_wquant, 1)
                dve.wait_ge(s_wquant, i + 1)

            dve.wait_ge(s_xhi, 1)
            nc.vector.tensor_tensor(xT[:, 1, :], TB1[:, 0:T], xT[:, 0, :], ALU.subtract).then_inc(s_xlo, 1)
            for j, k in enumerate("kvq"):
                dve.wait_ge(s_whi, j + 1)
                for hh in range(2):
                    hi, lo = (wmat[k][:, l].rearrange("p e (h m) -> p e h m", h=2)[:, :, hh] for l in range(2))
                    last = nc.vector.scalar_tensor_tensor(
                        out=lo, in0=split_src[k][:, :, hh], scalar=SCALE if k == "q" else 1.0, in1=hi,
                        op0=ALU.mult, op1=ALU.subtract)
                last.then_inc(s_wlo, 1)
            dve.wait_ge(s_whi, 4)
            nc.vector.tensor_tensor(w_o[:, 1, :], stage["o"], w_o[:, 0, :], ALU.subtract).then_inc(s_wlo, 1)
            dve.wait_ge(s_wlo, 4)
            dve.wait_ge(s_wT, 1)
            nc.vector.memset(q_bd[:, :].bitcast(F32), 0.0)
            nc.vector.memset(vst[:, 0, :, :, HALF:VW], 1.0)
            nc.vector.memset(vst[:, 1, :, :, HALF:VW], 0.0)

            def k_add(n, c):
                dve.wait_ge(s_done["k"], n * NC + c + 1)
                if c == 1:
                    dve.wait_ge(s_kfirst, n + 1)
                else:
                    dve.wait_ge(s_read["k"], n * PER["k"] + c - 1)
                acc = k_acc[:, :]
                nc.vector.scalar_tensor_tensor(out=acc, in0=slot_cols(("k", c)).rearrange("p e t -> p (e t)"), scalar=0.0,
                                               in1=acc, op0=ALU.max, op1=ALU.add).then_inc(s_read["k"], 1)

            def v_lo(n, c):
                dve.wait_ge(s_vhi, n * NC + c + 1)
                hi, lo = (vst[:, l].rearrange("p b s e -> p e (b s)")[:, c * EC:(c + 1) * EC] for l in range(2))
                nc.vector.tensor_tensor(lo, slot_cols(("v", c)), hi, ALU.subtract).then_inc(s_read["v"], 1)

            def q_scale(n, c, fresh):
                dve.wait_ge(s_done["q"], n * NC + c + 1)
                if not fresh:
                    dve.wait_ge(s_qlo, n * NC + c + 1 - QR)
                nc.vector.scalar_tensor_tensor(
                    out=q32[:, c % QR, :].rearrange("p (e t) -> p e t", t=T), in0=slot_cols(("q", c)), scalar=0.0,
                    in1=ks[:, :].unsqueeze(1).to_broadcast([P, EC, T]), op0=ALU.max, op1=ALU.mult
                ).then_inc(s_read["q"], 1)

            def normalise(o, g, fresh):
                i = o * NG + g + 1
                src = slot_cols(("out", g))
                dve.wait_ge(s_done["out"], i)
                nc.vector.tensor_scalar(nrm[:, g % 2, :], src[:, :, HALF], EPS_NORM, None, ALU.add).then_inc(s_nrm, 1)
                dve.wait_ge(s_nrm, i)
                nc.vector.reciprocal(rec[:, g % 2, :], nrm[:, g % 2, :]).then_inc(s_rec, 1)
                dve.wait_ge(s_rec, i)
                if not fresh:
                    dve.wait_ge(s_olo, i - OR)
                nc.vector.tensor_tensor(
                    o32[:, g % OR, :].rearrange("p (s b e) -> p s b e", b=2, e=HALF),
                    src[:, :, 0:PW].rearrange("p s (b e) -> p s b e", b=2)[:, :, :, 0:HALF],
                    rec[:, g % 2, :].unsqueeze(2).unsqueeze(3).to_broadcast([P, G, 2, HALF]),
                    ALU.mult).then_inc(s_read["out"], 1)

            def quantise(a, coarse, fine, chain, base, s_done_):
                n_ = 0
                for dst, ks_ in ((coarse, (6, 5, 4)), (fine, (0, 1, 2, 3))):
                    for k in ks_:
                        if k == ks_[0]:
                            ins = (nc.vector.tensor_scalar(dst, a, MIDS[k], 2.0, ALU.is_gt, ALU.mult) if k == 6
                                   else nc.vector.tensor_scalar(dst, a, MIDS[k], None, ALU.is_gt))
                        else:
                            ins = nc.vector.scalar_tensor_tensor(out=dst, in0=a, scalar=MIDS[k], in1=dst,
                                                                 op0=ALU.is_gt, op1=ALU.add)
                        ins.then_inc(chain, 1)
                        n_ += 1
                        dve.wait_ge(chain, base + n_)
                        yield
                nc.vector.scalar_tensor_tensor(out=fine, in0=fine, scalar=0.5, in1=coarse, op0=ALU.mult,
                                               op1=ALU.add).then_inc(s_done_, 1)
                yield

            def run(gen, count):
                for _ in range(count):
                    next(gen)

            def iteration(n):
                front, more, attend, mid, back = parts(n)
                o, m, b = n - 1, n - 2, n - 3
                first = isinstance(n, int) and n == 0
                if back:
                    dve.wait_ge(s_sig, b + 1)
                    nc.vector.tensor_tensor(sig[:, :], TB0[:, 0:FFN], sig[:, :], ALU.mult).then_inc(s_gs, 1)
                    dve.wait_ge(s_gs, b + 1)
                    dve.wait_ge(s_up, b + 1)
                    nc.vector.tensor_tensor(h[:, :], TB1[:, 0:FFN], sig[:, :], ALU.mult).then_inc(s_h, 1)
                    dve.wait_ge(s_h, b + 1)
                if front:
                    k_add(n, 1)
                if back:
                    nc.vector.tensor_reduce(hsc[:, 1, :], blocks(h[:, :]), AX.X, ALU.max,
                                            apply_absolute_value=True).then_inc(s_hmax, 1)
                    dve.wait_ge(s_hmax, b + 1)
                    nc.vector.tensor_scalar(hsc[:, 0, :], hsc[:, 1, :], 1.0 / 6.0, 1e-12, ALU.mult,
                                            ALU.max).then_inc(s_hsc, 1)
                    dve.wait_ge(s_hsc, b + 1)
                    nc.vector.reciprocal(hsc[:, 1, :], hsc[:, 0, :]).then_inc(s_hrs, 1)
                if front:
                    k_add(n, 2)
                if back:
                    dve.wait_ge(s_hrs, b + 1)
                    dve.wait_ge(s_habs, b + 1)
                    nc.vector.tensor_tensor(blocks(ha[:, :]), blocks(ha[:, :]), per_block(hsc[:, 1, :], h[:, :]),
                                            ALU.mult).then_inc(s_ha, 1)
                if front:
                    k_add(n, 3)
                    dve.wait_ge(s_read["k"], (n + 1) * PER["k"])
                    for i in range(3):
                        w = EC * T >> (i + 1)
                        nc.vector.tensor_tensor(k_acc[:, 0:w], k_acc[:, 0:w], k_acc[:, w:2 * w],
                                                ALU.add).then_inc(s_tree, 1)
                        dve.wait_ge(s_tree, n * 3 + i + 1)
                if back:
                    dve.wait_ge(s_ha, b + 1)
                    hquant = quantise(ha[:, :], hc[:, :], hq[:, :], s_hc, b * 7, s_hs)
                    run(hquant, 8)
                if mid:
                    dve.wait_ge(s_y, m + 1)
                    dve.wait_ge(s_xb, m + 1)
                    nc.vector.tensor_tensor(r1[:, :], TB0[:, 0:DIM], x_res[:, :], ALU.add).then_inc(s_r1, 1)
                    dve.wait_ge(s_r1, m + 1)
                    nc.vector.bn_stats(st1[:, :], r1[:, :]).then_inc(s_st1, 1)
                    dve.wait_ge(s_st1, m + 1)
                if attend:
                    normalise(o, 0, isinstance(n, int) and n == 1)
                if mid:
                    nc.vector.bn_aggr(mv1[:, :], st1[:, :]).then_inc(s_agg1, 1)
                if attend:
                    normalise(o, 1, isinstance(n, int) and n == 1)
                if mid:
                    dve.wait_ge(s_rs1, m + 1)
                    if back:
                        dve.wait_ge(s_x1b, b + 1)
                    nc.vector.tensor_scalar(x1[:, :], r1[:, :], mv1[:, 0:1], rs1[:, 0:1], ALU.subtract,
                                            ALU.mult).then_inc(s_x1, 1)
                    dve.wait_ge(s_x1, m + 1)
                    nc.vector.tensor_reduce(xsc[:, 1, :], blocks(x1[:, :]), AX.X, ALU.max,
                                            apply_absolute_value=True).then_inc(s_xmax, 1)
                    dve.wait_ge(s_xmax, m + 1)
                    nc.vector.tensor_scalar(xsc[:, 0, :], xsc[:, 1, :], 1.0 / 6.0, 1e-12, ALU.mult,
                                            ALU.max).then_inc(s_xsc, 1)
                    dve.wait_ge(s_xsc, m + 1)
                    nc.vector.reciprocal(xsc[:, 1, :], xsc[:, 0, :]).then_inc(s_xrs, 1)
                if mid:
                    dve.wait_ge(s_xrs, m + 1)
                    dve.wait_ge(s_xabs, m + 1)
                    nc.vector.tensor_tensor(blocks(xa[:, :]), blocks(xa[:, :]), per_block(xsc[:, 1, :], x1[:, :]),
                                            ALU.mult).then_inc(s_xa, 1)
                if attend:
                    normalise(o, 2, isinstance(n, int) and n == 1)
                if mid:
                    dve.wait_ge(s_xa, m + 1)
                    xquant = quantise(xa[:, :], xc[:, :], xq[:, :], s_xc, m * 7, s_xs)
                    run(xquant, 2)
                for g in range(3, NG):
                    if attend:
                        normalise(o, g, isinstance(n, int) and n == 1 and g < OR)
                    if mid and g < 6:
                        run(xquant, 2)
                if front:
                    v_lo(n, 0)
                    v_lo(n, 1)
                if back:
                    dve.wait_ge(s_dn, b + 1)
                    nc.vector.tensor_tensor(r2[:, :], TB0[:, 0:DIM], x1b[:, :], ALU.add).then_inc(s_r2, 1)
                    dve.wait_ge(s_r2, b + 1)
                    nc.vector.bn_stats(st2[:, :], r2[:, :]).then_inc(s_st2, 1)
                    dve.wait_ge(s_st2, b + 1)
                if front:
                    v_lo(n, 2)
                if back:
                    nc.vector.bn_aggr(mv2[:, :], st2[:, :]).then_inc(s_agg2, 1)
                if front:
                    v_lo(n, 3)
                    dve.wait_ge(s_ks, n + 1)
                if back:
                    dve.wait_ge(s_rs2, b + 1)
                    dve.wait_ge(s_store, 16 * (b + 1))
                    nc.vector.tensor_scalar(y_out[:, :], r2[:, :], mv2[:, 0:1], rs2[:, 0:1], ALU.subtract,
                                            ALU.mult).then_inc(s_yo, 1)
                if front:
                    for c in range(NC):
                        q_scale(n, c, first)
                if more:
                    dve.wait_ge(s_xhi, n + 2)
                    nc.vector.tensor_tensor(xT[:, 1, :], TB1[:, 0:T], xT[:, 0, :], ALU.subtract).then_inc(s_xlo, 1)

            run_tiles(dve, iteration)

        @block.gpsimd
        def _(pool):
            nc.gpsimd.memset(ident[:, :], 0.0)
            nc.gpsimd.memset(both[:, :], 0.0).then_inc(s_iota, 1)
            pool.wait_ge(s_iota, 2)
            nc.gpsimd.affine_select(out=ident[:, :], in_=ident[:, :], compare_op=ALU.not_equal, fill=1.0, base=0,
                                    pattern=[[-1, P]], channel_multiplier=1)
            for i, base in enumerate((0, -DH, DH)):
                ins = nc.gpsimd.affine_select(out=both[:, :], in_=both[:, :], compare_op=ALU.not_equal, fill=1.0,
                                              base=base, pattern=[[-1, P]], channel_multiplier=1)
                if i < 2:
                    ins.then_inc(s_iota, 1)
                    pool.wait_ge(s_iota, 3 + i)
            ins.then_inc(s_const, 1)
            pool.wait_ge(s_store, 16)

            def q_lo(n, c):
                pool.wait_ge(s_qhi, n * NC + c + 1)
                e = slice(c * EC, (c + 1) * EC)
                nc.gpsimd.tensor_tensor(qnat[:, 1, :, e, :], q32[:, c % QR, :].rearrange("p (e a s) -> p a e s", a=2, s=S),
                                        qnat[:, 0, :, e, :], ALU.subtract).then_inc(s_qlo, 1)

            def o_lo(o, g):
                pool.wait_ge(s_ohi, o * NG + g + 1)
                hi, lo = (ost[:, l, :, g * G:(g + 1) * G, :].rearrange("p b s e -> p s b e") for l in range(2))
                nc.gpsimd.tensor_tensor(lo, o32[:, g % OR, :].rearrange("p (s b e) -> p s b e", b=2, e=HALF), hi,
                                        ALU.subtract).then_inc(s_olo, 1)

            def rstd(t, agg, mv, ve, rs, s_ve, s_rs):
                pool.wait_ge(agg, t + 1)
                nc.gpsimd.tensor_tensor(ve[:, :], mv[:, 1:2], consts[:, 1:2], ALU.add).then_inc(s_ve, 1)
                pool.wait_ge(s_ve, t + 1)
                nc.gpsimd.tensor_tensor(rs[:, :], ve[:, :], consts[:, 0:1], ALU.pow).then_inc(s_rs, 1)

            def iteration(n):
                front, more, attend, mid, back = parts(n)
                o, m, b = n - 1, n - 2, n - 3
                if back:
                    nc.gpsimd.tensor_copy(x1b[:, :], x1[:, :]).then_inc(s_x1b, 1)
                if mid:
                    pool.wait_ge(s_xres, (m + 1) * 16)
                    nc.gpsimd.tensor_tensor(x_res[:, :], x_res[:, :], bo_b[:, :], ALU.add).then_inc(s_xb, 1)
                if back:
                    pool.wait_ge(s_hsgn, b + 1)
                    pool.wait_ge(s_hsc, b + 1)
                    nc.gpsimd.tensor_tensor(blocks(hss[:, :]), blocks(hsgn[:, :]), per_block(hsc[:, 0, :], h[:, :]),
                                            ALU.mult).then_inc(s_hss, 1)
                    pool.wait_ge(s_hss, b + 1)
                    pool.wait_ge(s_hs, b + 1)
                    nc.gpsimd.tensor_tensor(hq[:, :], hq[:, :], hss[:, :], ALU.mult).then_inc(s_hq, 1)
                if mid:
                    rstd(m, s_agg1, mv1, ve1, rs1, s_ve1, s_rs1)
                if attend:
                    for g in range(3):
                        o_lo(o, g)
                if mid:
                    pool.wait_ge(s_xsgn, m + 1)
                    pool.wait_ge(s_xsc, m + 1)
                    nc.gpsimd.tensor_tensor(blocks(xsgn[:, :]), blocks(xsgn[:, :]), per_block(xsc[:, 0, :], x1[:, :]),
                                            ALU.mult).then_inc(s_xss, 1)
                if attend:
                    for g in range(3, NG):
                        o_lo(o, g)
                if mid:
                    pool.wait_ge(s_xss, m + 1)
                    pool.wait_ge(s_xs, m + 1)
                    nc.gpsimd.tensor_tensor(xq[:, :], xq[:, :], xsgn[:, :], ALU.mult).then_inc(s_xq, 1)
                if back:
                    rstd(b, s_agg2, mv2, ve2, rs2, s_ve2, s_rs2)
                if front:
                    for c in range(NC):
                        q_lo(n, c)

            run_tiles(pool, iteration)


_INS = ['L0_attn_x', 'L0_attn_Wq', 'L0_attn_Wk', 'L0_attn_Wv', 'L0_attn_Wo', 'L0_attn_bo', 'L0_ffn_w_gate',
        'L0_ffn_w_up', 'L0_ffn_w_down']


def kernel(**inputs):
    import numpy as _np
    import concourse.bacc as _bacc
    from concourse import mybir as _mybir
    from concourse.bass_utils import run_bass_kernel_spmd as _run

    nc = _bacc.Bacc("TRN2", target_bir_lowering=False, num_devices=1)
    arrays, args = {}, []
    for name in _INS:
        a = _np.ascontiguousarray(inputs[name])
        arrays[f"in_{name}"] = a
        args.append(nc.dram_tensor(f"in_{name}", a.shape, _mybir.dt.from_np(a.dtype), kind="ExternalInput").ap())
    shape = inputs['L0_attn_x'].shape
    args.append(nc.dram_tensor("out_0", tuple(shape), _mybir.dt.float32, kind="ExternalOutput").ap())
    attention_ffn(nc, *args)
    r = _run(nc, [arrays], core_ids=[0])
    return r.results[0]["out_0"]
```

```python
from contextlib import ExitStack

import concourse.bass as bass
from concourse import mybir

F32 = mybir.dt.float32
BF16 = mybir.dt.bfloat16
ALU = mybir.AluOpType
ACT = mybir.ActivationFunctionType
AX = mybir.AxisListType

P = 128
DIM = 128
HEADS = 64
DH = 64
HALF = DH // 2
T = 128
S = T // 2
VW = HALF + 1
PW = 2 * VW
FFN = 352
BLK = 16
EPS_NORM = 1e-6
EPS_LN = 1e-5
SCALE = DH ** -0.5

EC = 8
NC = HALF // EC
G = 8
NG = S // G
SLOTS = 3
QR = 4
OR = 4
NR = 4
MIDS = [0.25, 0.75, 1.25, 1.75, 2.5, 3.5, 5.0]
KSUM_AT = 24
GU_BANK = 2 * (SLOTS - 1)
WP = 88
DOWN = [(0, 128), (128, 128), (256, 96)]

USES = ([("k", c) for c in range(NC)]
        + [u for c in range(NC) for u in (("q", c), ("out", 2 * c), ("out", 2 * c + 1))]
        + [("v", c) for c in range(NC)])
SLOT = {u: i % SLOTS for i, u in enumerate(USES)}


def attention_ffn(nc, x, wq, wk, wv, wo, bo, w_gate, w_up, w_down, out):
    NT = x.shape[0] * x.shape[1] // T
    x_t = x.rearrange("b s c -> (b s) c")
    out_t = out.rearrange("b s c -> (b s) c")

    ctx = ExitStack()
    with ctx:
        def sb(name, shape, dt=F32):
            return ctx.enter_context(nc.sbuf_tensor(name, shape, dt))

        def sem(name):
            return ctx.enter_context(nc.semaphore(name))

        w_kvq = {k: sb(f"w_{k}", [P, 2, HALF * P], BF16) for k in "kvq"}
        w_o = sb("w_o", [P, 2, HALF * DIM], BF16)
        w_gu = sb("w_gu", [P, 2 * FFN])
        w_dn = sb("w_dn", [P, 3, DIM])
        k_acc = sb("k_acc", [P, EC * T])
        ks = sb("ks", [P, T])
        q32 = sb("q32", [P, QR, EC * T])
        q_nat = sb("q_nat", [P, 2 * 2 * HALF * S], BF16)
        q_bd = sb("q_bd", [P, 2 * 2 * DH * S], BF16)
        v_st = sb("v_st", [P, 2 * 2 * S * VW], BF16)
        o_st = sb("o_st", [P, 2 * 2 * S * HALF], BF16)
        swap = sb("swap", [P, 2 * S * VW], BF16)
        o32 = sb("o32", [P, OR, G * DH])
        nrm = sb("nrm", [P, NR, G])
        rec = sb("rec", [P, NR, G])
        xk = sb("xk", [P, 2, T], BF16)
        xT = sb("xT", [P, 2, T], BF16)
        x_in = sb("x_in", [T, DIM])
        x_res = sb("x_res", [T, DIM])
        bo_b = sb("bo_b", [P, DIM])
        ident = sb("ident", [P, P])
        both = sb("both", [P, P])
        warm = sb("warm", [P, 1])
        consts = sb("consts", [P, 2])
        r1, x1, xa, xsgn, xc, xq = (sb(v, [T, DIM]) for v in ("r1", "x1", "xa", "xsgn", "xc", "xq"))
        xqT = sb("xqT", [P, T])
        xsc = sb("xsc", [T, 2, DIM // BLK])
        sig, h, ha, hc, hq, hss = (sb(v, [T, FFN]) for v in ("sig", "h", "ha", "hc", "hq", "hss"))
        hsgn = sb("hsgn", [T, FFN], BF16)
        hsc = sb("hsc", [T, 2, FFN // BLK])
        hqT = sb("hqT", [P, 3, T])
        x1b, r2, y_out = (sb(v, [T, DIM]) for v in ("x1b", "r2", "y_out"))
        st1, st2 = sb("st1", [T, 6]), sb("st2", [T, 6])
        mv1, mv2 = sb("mv1", [T, 2]), sb("mv2", [T, 2])
        ve1, rs1, ve2, rs2 = (sb(v, [T, 1]) for v in ("ve1", "rs1", "ve2", "rs2"))

        ps = ctx.enter_context(nc.psum_tensor("ps", [P, 8, 512], F32))
        TB0, TB1 = ps[:, 2 * SLOTS, :], ps[:, 2 * SLOTS + 1, :]

        def slot_cols(u):
            k = 2 * SLOT[u]
            return ps[:, k:k + 2, :].rearrange("p b (e t) -> p (b e) t", t=P)

        qbd = q_bd[:, :].rearrange("p (l c m s) -> p l c m s", l=2, c=2, s=S)
        qmat = q_bd[:, :].rearrange("p (l m s) -> p l m s", l=2, s=S)
        qnat = q_nat[:, :].rearrange("p (l a e s) -> p l a e s", l=2, a=2, s=S)
        vst = v_st[:, :].rearrange("p (l b s e) -> p l b s e", l=2, b=2, s=S)
        ost = o_st[:, :].rearrange("p (l b s e) -> p l b s e", l=2, b=2, s=S)
        omat = o_st[:, :].rearrange("p (l t e) -> p l t e", l=2, t=T)
        wmat = {k: w_kvq[k][:, :, :].rearrange("p l (e m) -> p l e m", m=P) for k in "kvq"}
        womat = w_o[:, :, :].rearrange("p l (e n) -> p l e n", n=DIM)

        stage = {"k": q_bd[:, 0:8192].bitcast(F32), "v": q_bd[:, 8192:16384].bitcast(F32),
                 "q": q32[:, :, :].rearrange("p r e -> p (r e)"), "o": q_nat[:, :].bitcast(F32)}
        gu_raw, gu_abs, gu_q, gu_m = (v_st[:, i * 2048:(i + 1) * 2048].bitcast(F32) for i in range(4))
        dn_raw, dn_abs, dn_q, dn_m = (o_st[:, i * 704:(i + 1) * 704].bitcast(F32) for i in range(4))
        w_sc = o_st[:, 2816:3072].bitcast(F32)
        split_src = {k: stage[k].rearrange("p (h i d) -> p i h d", h=2, i=HALF) for k in "kvq"}

        s_wload = {k: sem(f"s_wload_{k}") for k in "kvqo"}
        s_whi = {k: sem(f"s_whi_{k}") for k in "kvqo"}
        s_wlo = {k: sem(f"s_wlo_{k}") for k in "kvqo"}
        s_fload, s_const, s_wstep, s_wquant, s_wT, s_ffnw, s_iota, s_clear = (
            sem(f"s_{v}") for v in "fload const wstep wquant wT ffnw iota clear".split())
        s_x = sem("s_x")
        s_xps = sem("s_xps")
        s_xhi, s_xlo, s_xcopy = sem("s_xhi"), sem("s_xlo"), sem("s_xcopy")
        s_done = {k: sem(f"s_done_{k}") for k in ("k", "v", "q", "out")}
        s_read = {k: sem(f"s_read_{k}") for k in ("k", "v", "q", "out")}
        s_kfirst = sem("s_kfirst")
        s_tree = sem("s_tree")
        s_ksps, s_ks = sem("s_ksps"), sem("s_ks")
        s_vhi, s_qhi, s_qlo = sem("s_vhi"), sem("s_qhi"), sem("s_qlo")
        s_vswap, s_qbd, s_qstay = [sem("s_vswap_hi"), sem("s_vswap_lo")], sem("s_qbd"), sem("s_qstay")
        s_nrm, s_rec = sem("s_nrm"), sem("s_rec")
        s_ohi, s_olo, s_oswap = sem("s_ohi"), sem("s_olo"), [sem("s_oswap_hi"), sem("s_oswap_lo")]
        (s_xres, s_xb, s_y, s_r1, s_st1, s_agg1, s_ve1, s_rs1, s_x1, s_xabs, s_xmax, s_xsc, s_xrs, s_xa, s_xc, s_xs,
         s_xsgn, s_xss, s_xq, s_xqps, s_xqT, s_gate, s_up, s_sig, s_gs, s_h) = (sem(f"s_{v}") for v in (
             "xres xb y r1 st1 agg1 ve1 rs1 x1 xabs xmax xsc xrs xa xc xs xsgn xss xq xqps xqT gate up sig gs h").split())
        (s_habs, s_hmax, s_hsc, s_hrs, s_ha, s_hc, s_hs, s_hsgn, s_hss, s_hq, s_hps, s_hqT, s_dn, s_x1b, s_r2, s_st2, s_agg2,
         s_ve2, s_rs2, s_yo, s_store) = (sem(f"s_{v}") for v in (
             "habs hmax hsc hrs ha hc hs hsgn hss hq hps hqT dn x1b r2 st2 agg2 ve2 rs2 yo store").split())

        PER = {"k": NC - 1, "v": NC, "q": NC, "out": NG}

        def slot_read(it, u):
            kind, c = u
            if u == ("k", 0):
                return s_kfirst, it + 1
            return s_read[kind], (it - 1 if kind == "out" else it) * PER[kind] + (c if kind == "k" else c + 1)

        def wait_slot(pe, it, u):
            i = USES.index(u)
            for back in range(1, 3 * len(USES)):
                j = i - back
                w, wit = USES[j % len(USES)], it + j // len(USES)
                if SLOT[w] != SLOT[u]:
                    continue
                if isinstance(it, int):
                    tile_of = wit - (w[0] == "out")
                    if wit < 0:
                        return
                    if not 0 <= tile_of < NT:
                        continue
                pe.wait_ge(*slot_read(wit, w))
                return

        def run_tiles(eng, iteration):
            for n in range(3):
                iteration(n)
            with eng.Fori(3, NT - 1) as n:
                iteration(n)
            for n in range(NT - 1, NT + 3):
                iteration(n)

        def parts(n):
            if not isinstance(n, int):
                return True, True, True, True, True
            return n < NT, n + 1 < NT, 0 <= n - 1 < NT, 0 <= n - 2 < NT, 0 <= n - 3 < NT

        block = ctx.enter_context(nc.Block())

        @block.sync
        def _(sp):
            gu = gu_raw.rearrange("p (g q k) -> p g q k", g=2, k=DIM)
            for g, w in enumerate((w_gate, w_up)):
                sp.dma_start(gu[0:WP, g], w.rearrange("(q p) k -> p q k", p=WP)).then_inc(s_fload, 16)
            sp.dma_start(dn_raw, w_down).then_inc(s_fload, 16)
            sp.dma_start(x_in[:, :], x_t[0:T, :]).then_inc(s_x, 16)
            for k, w in (("k", wk), ("v", wv), ("q", wq)):
                sp.dma_start(stage[k], w).then_inc(s_wload[k], 16)
            for j in range(2):
                sp.dma_start(stage["o"][j * HEADS:(j + 1) * HEADS, :],
                             wo.rearrange("(i j e) n -> j i (e n)", j=2, e=HALF)[j]).then_inc(s_wload["o"], 16)
            sp.dma_start(bo_b[:, :], bo.partition_broadcast(P)).then_inc(s_store, 16)

            osw = swap[0:64, 0:2 * S * HALF].rearrange("p (l e) -> p l e", l=2)
            vsw = swap[64:128, :].rearrange("p (l e) -> p l e", l=2)
            o4 = o_st[:, :].rearrange("p (l b e) -> p l b e", l=2, b=2)
            v4 = v_st[:, :].rearrange("p (l b e) -> p l b e", l=2, b=2)

            def move(l, blocks4, stage_, sems, tile, step):
                dst, src = ((stage_[:, l], blocks4[64:128, l, 0]), (blocks4[64:128, l, 0], blocks4[0:64, l, 1]),
                            (blocks4[0:64, l, 1], stage_[:, l]))[step]
                if step:
                    sp.wait_ge(sems[l], tile * 48 + 16 * step)
                sp.dma_start(dst, src).then_inc(sems[l], 16)

            def q_move(n, l, par):
                e = (1 - par) * HALF
                sp.dma_start(qbd[par * 64:par * 64 + 64, l, par, e:e + HALF],
                             qnat[e * 2:e * 2 + 64, l, par]).then_inc(s_qbd, 16)

            def iteration(n):
                front, more, attend, mid, back = parts(n)
                o = n - 1
                if more:
                    sp.wait_ge(s_xps, n + 1)
                    sp.dma_start(x_in[:, :], x_t[bass.ts(n + 1, T), :]).then_inc(s_x, 16)
                if attend:
                    if mid:
                        sp.wait_ge(s_r1, n - 1)
                    sp.dma_start(x_res[:, :], x_t[bass.ts(o, T), :]).then_inc(s_xres, 16)
                    sp.wait_ge(s_ohi, (o + 1) * NG)
                    move(0, o4, osw, s_oswap, o, 0)
                    sp.wait_ge(s_olo, (o + 1) * NG)
                    move(1, o4, osw, s_oswap, o, 0)
                if front:
                    sp.wait_ge(s_qhi, (n + 1) * NC)
                    if isinstance(n, int) and n == 0:
                        sp.wait_ge(s_clear, 2)
                    q_move(n, 0, 0)
                if attend:
                    move(0, o4, osw, s_oswap, o, 1)
                if front:
                    q_move(n, 0, 1)
                if attend:
                    move(1, o4, osw, s_oswap, o, 1)
                if front:
                    sp.wait_ge(s_vhi, (n + 1) * NC)
                    move(0, v4, vsw, s_vswap, n, 0)
                    sp.wait_ge(s_read["v"], (n + 1) * NC)
                    move(1, v4, vsw, s_vswap, n, 0)
                if attend:
                    move(0, o4, osw, s_oswap, o, 2)
                    move(1, o4, osw, s_oswap, o, 2)
                if front:
                    move(0, v4, vsw, s_vswap, n, 1)
                    move(1, v4, vsw, s_vswap, n, 1)
                    sp.wait_ge(s_qlo, (n + 1) * NC)
                    q_move(n, 1, 0)
                    q_move(n, 1, 1)
                    move(0, v4, vsw, s_vswap, n, 2)
                    move(1, v4, vsw, s_vswap, n, 2)
                if back:
                    sp.wait_ge(s_yo, n - 2)
                    sp.dma_start(out_t[bass.ts(n - 3, T), :], y_out[:, :]).then_inc(s_store, 16)

            run_tiles(sp, iteration)
            sp.wait_ge(s_store, 16 * (NT + 1))

        @block.tensor
        def _(pe):
            pe.wait_ge(s_const, 1)
            pe.wait_ge(s_x, 16)
            nc.tensor.transpose(TB1[:, 0:T], x_in[:, :], ident[:, :]).then_inc(s_xps, 1)
            pe.wait_ge(s_wquant, 1)
            gq = gu_q.rearrange("p (g k) -> p g k", k=DIM)
            for g in range(8):
                last = nc.tensor.transpose(ps[:, GU_BANK + g // 4, (g % 4) * WP:(g % 4 + 1) * WP], gq[0:WP, g, :],
                                           ident[0:WP, 0:WP])
            last.then_inc(s_wT, 1)

            def transpose_down_weights():
                pe.wait_ge(s_wquant, 2)
                for c, (k0, kn) in enumerate(DOWN):
                    last = nc.tensor.transpose(TB0[0:kn, c * DIM:(c + 1) * DIM], dn_q[:, k0:k0 + kn], ident[:, :])
                last.then_inc(s_wT, 1)

            def three(dst, lhs, rhs):
                nc.tensor.matmul(dst, lhs(0), rhs(0), start=True, stop=False)
                nc.tensor.matmul(dst, lhs(0), rhs(1), start=False, stop=False)
                return nc.tensor.matmul(dst, lhs(1), rhs(0), start=False, stop=True)

            def project(n, kind, c):
                wait_slot(pe, n, (kind, c))
                dst = slot_cols((kind, c))
                xin = xk if kind == "k" else xT
                for e in range(EC):
                    last = three(dst[:, e, :], lambda l: wmat[kind][:, l, c * EC + e, :], lambda l: xin[:, l, :])
                last.then_inc(s_done[kind], 1)

            def out_group(n, g):
                wait_slot(pe, n, ("out", g))
                dst = slot_cols(("out", g))
                for p in range(G):
                    s = g * G + p
                    last = three(dst[:, p, 0:PW], lambda l: qmat[:, l, :, s], lambda l: vst[:, l, :, s, :])
                last.then_inc(s_done["out"], 1)

            def sum_halves(n, ready):
                pe.wait_ge(s_tree, (n + 1) * 3)
                if ready:
                    pe.wait_ge(s_h, n - 2)
                nc.tensor.matmul(TB1[:, 0:T], both[:, :], k_acc[:, 0:T], start=True, stop=True).then_inc(s_ksps, 1)

            def wo_projection(m, first, front, back):
                pe.wait_ge(s_oswap[0], (m + 1) * 48)
                pe.wait_ge(s_oswap[1], (m + 1) * 48)
                if not first:
                    pe.wait_ge(s_gs, m)
                for j in range(HALF):
                    if front and j == KSUM_AT:
                        sum_halves(m + 2, back)
                    for i, (lo, lw) in enumerate(((0, 0), (0, 1), (1, 0))):
                        last = nc.tensor.matmul(TB0[:, 0:DIM], omat[:, lo, :, j], womat[:, lw, j, :],
                                                start=(j == 0 and i == 0), stop=(j == HALF - 1 and i == 2))
                last.then_inc(s_y, 1)

            def transpose_h(b):
                pe.wait_ge(s_hq, b + 1)
                for c, (k0, kn) in enumerate(DOWN):
                    last = nc.tensor.transpose(TB1[0:kn, c * T:(c + 1) * T], hq[:, k0:k0 + kn], ident[:, :])
                last.then_inc(s_hps, 1)

            def down_projection(b, mid):
                pe.wait_ge(s_hqT, b + 1)
                if mid:
                    pe.wait_ge(s_r1, b + 2)
                for c, (k0, kn) in enumerate(DOWN):
                    last = nc.tensor.matmul(TB0[:, 0:DIM], hqT[0:kn, c, :], w_dn[0:kn, c, :],
                                            start=(c == 0), stop=(c == len(DOWN) - 1))
                last.then_inc(s_dn, 1)

            def gate_up(m, more, back):
                pe.wait_ge(s_xqT, m + 1)
                if more:
                    pe.wait_ge(s_xlo, m + 4)
                elif back:
                    pe.wait_ge(s_r2, m)
                nc.tensor.matmul(TB0[:, 0:FFN], xqT[:, :], w_gu[:, 0:FFN], start=True, stop=True).then_inc(s_gate, 1)
                nc.tensor.matmul(TB1[:, 0:FFN], xqT[:, :], w_gu[:, FFN:2 * FFN],
                                 start=True, stop=True).then_inc(s_up, 1)

            def iteration(n):
                front, more, attend, mid, back = parts(n)
                m, b = n - 2, n - 3
                if front:
                    pe.wait_ge(s_xlo, n + 1)
                    first = isinstance(n, int) and n == 0
                    if first:
                        pe.wait_ge(s_wlo["k"], 1)
                    for c in range(NC):
                        if first and c == SLOTS - 1:
                            pe.wait_ge(s_ffnw, 1)
                        if first and c == SLOTS:
                            transpose_down_weights()
                        project(n, "k", c)
                    pe.wait_ge(s_xcopy, n + 1)
                    if first:
                        pe.wait_ge(s_wlo["q"], 1)
                    project(n, "q", 0)
                if mid:
                    if not back:
                        pe.wait_ge(s_wlo["o"], 1)
                    wo_projection(m, not back, front, back)
                elif front:
                    sum_halves(n, back)
                for c in range(NC):
                    if front and c:
                        project(n, "q", c)
                    if back and c == 1:
                        if front:
                            pe.wait_ge(s_ks, n + 1)
                        transpose_h(b)
                    if attend:
                        if c == 0:
                            pe.wait_ge(s_qbd, n * 64)
                            pe.wait_ge(s_qstay, n * 4)
                            pe.wait_ge(s_vswap[0], n * 48)
                            pe.wait_ge(s_vswap[1], n * 48)
                        out_group(n, 2 * c)
                        out_group(n, 2 * c + 1)
                    if back and c == 2:
                        down_projection(b, mid)
                if front:
                    if first:
                        pe.wait_ge(s_wlo["v"], 1)
                    project(n, "v", 0)
                if more:
                    pe.wait_ge(s_x, (n + 2) * 16)
                    if back:
                        pe.wait_ge(s_r2, b + 1)
                    elif mid:
                        pe.wait_ge(s_r1, m + 1)
                    elif attend:
                        pe.wait_ge(s_xlo, n + 1)
                    else:
                        pe.wait_ge(s_ffnw, 2)
                    nc.tensor.transpose(TB0[:, 0:T], x_in[:, :], ident[:, :]).then_inc(s_xps, 1)
                if front:
                    project(n, "v", 1)
                    project(n, "v", 2)
                if mid:
                    pe.wait_ge(s_xq, m + 1)
                    if front and not back:
                        pe.wait_ge(s_ks, n + 1)
                    nc.tensor.transpose(TB1[:, 0:T], xq[:, :], ident[:, :]).then_inc(s_xqps, 1)
                if front:
                    project(n, "v", 3)
                if mid:
                    gate_up(m, more, back)

            run_tiles(pe, iteration)

        @block.scalar
        def _(act):
            act.wait_ge(s_xps, 1)
            nc.scalar.copy(xk[:, 0, :], TB1[:, 0:T]).then_inc(s_xhi, 1)

            def weight_hi(k):
                act.wait_ge(s_wload[k], 16)
                nc.scalar.activation(wmat[k][:, 0].rearrange("p e (h m) -> p e h m", h=2), split_src[k], ACT.Copy,
                                     scale=SCALE if k == "q" else 1.0).then_inc(s_whi[k], 1)

            weight_hi("k")
            weight_hi("v")
            act.wait_ge(s_wT, 1)
            nc.scalar.copy(w_gu[:, :].rearrange("p (g n) -> p g n", g=2),
                           ps[:, GU_BANK:GU_BANK + 2, 0:FFN]).then_inc(s_ffnw, 1)
            weight_hi("q")
            act.wait_ge(s_wload["o"], 32)
            nc.scalar.copy(w_o[:, 0, :], stage["o"]).then_inc(s_whi["o"], 1)
            act.wait_ge(s_wT, 2)
            for c, (k0, kn) in enumerate(DOWN):
                last = nc.scalar.copy(w_dn[0:kn, c, :], TB0[0:kn, c * DIM:(c + 1) * DIM])
            last.then_inc(s_ffnw, 1)

            def v_hi(n, c):
                act.wait_ge(s_done["v"], n * NC + c + 1)
                dst = vst[:, 0].rearrange("p b s e -> p e (b s)")[:, c * EC:(c + 1) * EC]
                nc.scalar.copy(dst, slot_cols(("v", c))).then_inc(s_vhi, 1)

            def q_hi(n, c):
                act.wait_ge(s_read["q"], n * NC + c + 1)
                nc.scalar.copy(qnat[:, 0, :, c * EC:(c + 1) * EC, :],
                               q32[:, c % QR, :].rearrange("p (e a s) -> p a e s", a=2, s=S)).then_inc(s_qhi, 1)

            def q_stay(l, par):
                rows, e = slice(par * 64, par * 64 + 64), par * HALF
                nc.scalar.copy(qbd[rows, l, par, e:e + HALF], qnat[rows, l, par]).then_inc(s_qstay, 1)

            def o_hi(o, g):
                act.wait_ge(s_read["out"], o * NG + g + 1)
                nc.scalar.copy(ost[:, 0, :, g * G:(g + 1) * G, :].rearrange("p b s e -> p s b e"),
                               o32[:, g % OR, :].rearrange("p (s b e) -> p s b e", b=2, e=HALF)).then_inc(s_ohi, 1)

            def iteration(n):
                front, more, attend, mid, back = parts(n)
                o, m, b = n - 1, n - 2, n - 3
                if front:
                    act.wait_ge(s_done["k"], n * NC + 1)
                    nc.scalar.activation(k_acc[:, :].rearrange("p (e t) -> p e t", t=T), slot_cols(("k", 0)),
                                         ACT.Relu).then_inc(s_kfirst, 1)
                    act.wait_ge(s_xlo, n + 1)
                    nc.scalar.copy(xT[:, :, :], xk[:, :, :]).then_inc(s_xcopy, 1)
                if back:
                    act.wait_ge(s_h, b + 1)
                    nc.scalar.activation(ha[:, :], h[:, :], ACT.Abs).then_inc(s_habs, 1)
                    nc.scalar.activation(hsgn[:, :], h[:, :], ACT.Sign).then_inc(s_hsgn, 1)
                if attend:
                    if isinstance(n, int) and n == 1:
                        act.wait_ge(s_clear, 2)
                    act.wait_ge(s_qhi, n * NC)
                    q_stay(0, 0)
                    q_stay(0, 1)
                    act.wait_ge(s_qlo, (o + 1) * NC)
                    q_stay(1, 0)
                    q_stay(1, 1)
                if front:
                    act.wait_ge(s_ksps, n + 1)
                    nc.scalar.copy(ks[:, :], TB1[:, 0:T]).then_inc(s_ks, 1)
                if attend and mid:
                    act.wait_ge(s_y, m + 1)
                if mid:
                    nc.scalar.activation(warm[:, :], consts[:, 1:2], ACT.Sigmoid)
                if isinstance(n, int) and n == 0:
                    act.wait_ge(s_wlo["o"], 1)
                if attend and front:
                    act.wait_ge(s_qbd, n * 64)
                for c in range(NC):
                    if front:
                        q_hi(n, c)
                    if back and c == 1:
                        act.wait_ge(s_hps, b + 1)
                        for i, (k0, kn) in enumerate(DOWN):
                            last = nc.scalar.copy(hqT[0:kn, i, :], TB1[0:kn, i * T:(i + 1) * T])
                        last.then_inc(s_hqT, 1)
                    if attend:
                        o_hi(o, 2 * c)
                    if front and c == NC - 1:
                        v_hi(n, 0)
                    if attend:
                        o_hi(o, 2 * c + 1)
                    if mid and c == 0:
                        act.wait_ge(s_x1, m + 1)
                        nc.scalar.activation(xa[:, :], x1[:, :], ACT.Abs).then_inc(s_xabs, 1)
                        nc.scalar.activation(xsgn[:, :], x1[:, :], ACT.Sign).then_inc(s_xsgn, 1)
                if more:
                    act.wait_ge(s_xps, n + 2)
                    nc.scalar.copy(xk[:, 0, :], TB0[:, 0:T]).then_inc(s_xhi, 1)
                if front:
                    v_hi(n, 1)
                    v_hi(n, 2)
                if mid:
                    act.wait_ge(s_xqps, m + 1)
                    nc.scalar.copy(xqT[:, :], TB1[:, 0:T]).then_inc(s_xqT, 1)
                if front:
                    v_hi(n, 3)
                if mid:
                    act.wait_ge(s_gate, m + 1)
                    nc.scalar.activation(sig[:, :], TB0[:, 0:FFN], ACT.Sigmoid).then_inc(s_sig, 1)

            run_tiles(act, iteration)

        def blocks(a):
            return a.rearrange("p (b k) -> p b k", k=BLK)

        def per_block(a, like):
            return a.unsqueeze(2).to_broadcast([like.shape[0], like.shape[1] // BLK, BLK])

        @block.vector
        def _(dve):
            nc.vector.memset(consts[:, 0:1], -0.5)
            nc.vector.memset(consts[:, 1:2], EPS_LN).then_inc(s_iota, 1)
            steps = [0]

            def link(ins):
                steps[0] += 1
                ins.then_inc(s_wstep, 1)
                dve.wait_ge(s_wstep, steps[0])

            for i, (np_, raw, ab, q, mask) in enumerate(((WP, gu_raw, gu_abs, gu_q, gu_m), (P, dn_raw, dn_abs, dn_q, dn_m))):
                raw, ab, q, mask = raw[0:np_], ab[0:np_], q[0:np_], mask[0:np_]
                nb = raw.shape[1] // BLK
                sc, rs = w_sc[0:np_, 0:nb], w_sc[0:np_, 64:64 + nb]
                dve.wait_ge(s_fload, 48)
                link(nc.vector.tensor_reduce(sc, blocks(raw), AX.X, ALU.max, apply_absolute_value=True))
                link(nc.vector.tensor_scalar(sc, sc, 1.0 / 6.0, 1e-12, ALU.mult, ALU.max))
                link(nc.vector.reciprocal(rs, sc))
                link(nc.vector.scalar_tensor_tensor(out=ab, in0=raw, scalar=-1.0, in1=raw, op0=ALU.mult, op1=ALU.max))
                link(nc.vector.tensor_tensor(blocks(ab), blocks(ab), per_block(rs, raw), ALU.mult))
                link(nc.vector.tensor_scalar(q, ab, MIDS[6], 2.0, ALU.is_gt, ALU.mult))
                for k in (5, 4):
                    link(nc.vector.scalar_tensor_tensor(out=q, in0=ab, scalar=MIDS[k], in1=q, op0=ALU.is_gt, op1=ALU.add))
                link(nc.vector.tensor_scalar(mask, ab, MIDS[0], None, ALU.is_gt))
                for k in (1, 2, 3):
                    link(nc.vector.scalar_tensor_tensor(out=mask, in0=ab, scalar=MIDS[k], in1=mask, op0=ALU.is_gt,
                                                        op1=ALU.add))
                link(nc.vector.scalar_tensor_tensor(out=q, in0=mask, scalar=0.5, in1=q, op0=ALU.mult, op1=ALU.add))
                link(nc.vector.tensor_scalar(mask, raw, 0.0, 2.0, ALU.is_ge, ALU.mult))
                link(nc.vector.scalar_tensor_tensor(out=q, in0=mask, scalar=-1.0, in1=q, op0=ALU.add, op1=ALU.mult))
                nc.vector.tensor_tensor(blocks(q), blocks(q), per_block(sc, raw), ALU.mult).then_inc(s_wquant, 1)
                dve.wait_ge(s_wquant, i + 1)
                if i == 0:
                    dve.wait_ge(s_xhi, 1)
                    nc.vector.tensor_tensor(xk[:, 1, :], TB1[:, 0:T], xk[:, 0, :], ALU.subtract).then_inc(s_xlo, 1)

            dve.wait_ge(s_whi["q"], 1)
            for hh in range(2):
                hi, lo = (wmat["q"][:, l].rearrange("p e (h m) -> p e h m", h=2)[:, :, hh] for l in range(2))
                last = nc.vector.scalar_tensor_tensor(out=lo, in0=split_src["q"][:, :, hh], scalar=SCALE, in1=hi,
                                                      op0=ALU.mult, op1=ALU.subtract)
            last.then_inc(s_wlo["q"], 1)
            dve.wait_ge(s_wlo["q"], 1)

            def k_add(n, c):
                dve.wait_ge(s_done["k"], n * NC + c + 1)
                if c == 1:
                    dve.wait_ge(s_kfirst, n + 1)
                else:
                    dve.wait_ge(s_read["k"], n * PER["k"] + c - 1)
                acc = k_acc[:, :]
                nc.vector.scalar_tensor_tensor(out=acc, in0=slot_cols(("k", c)).rearrange("p e t -> p (e t)"), scalar=0.0,
                                               in1=acc, op0=ALU.max, op1=ALU.add).then_inc(s_read["k"], 1)

            def v_lo(n, c):
                dve.wait_ge(s_vhi, n * NC + c + 1)
                hi, lo = (vst[:, l].rearrange("p b s e -> p e (b s)")[:, c * EC:(c + 1) * EC] for l in range(2))
                nc.vector.tensor_tensor(lo, slot_cols(("v", c)), hi, ALU.subtract).then_inc(s_read["v"], 1)

            def q_scale(n, c, fresh):
                dve.wait_ge(s_done["q"], n * NC + c + 1)
                if not fresh:
                    dve.wait_ge(s_qlo, n * NC + c + 1 - QR)
                nc.vector.scalar_tensor_tensor(
                    out=q32[:, c % QR, :].rearrange("p (e t) -> p e t", t=T), in0=slot_cols(("q", c)), scalar=0.0,
                    in1=ks[:, :].unsqueeze(1).to_broadcast([P, EC, T]), op0=ALU.max, op1=ALU.mult
                ).then_inc(s_read["q"], 1)

            def norm_o(o, g):
                dve.wait_ge(s_done["out"], o * NG + g + 1)
                nc.vector.tensor_scalar(nrm[:, g % NR, :], slot_cols(("out", g))[:, :, HALF], EPS_NORM, None,
                                        ALU.add).then_inc(s_nrm, 1)

            def recip(o, g, count):
                dve.wait_ge(s_nrm, o * NG + g + count)
                r = slice(g % NR, g % NR + count)
                nc.vector.reciprocal(rec[:, r, :], nrm[:, r, :]).then_inc(s_rec, count)

            def scale_o(o, g, fresh):
                i = o * NG + g + 1
                dve.wait_ge(s_rec, i)
                if not fresh:
                    dve.wait_ge(s_olo, i - OR)
                nc.vector.tensor_tensor(
                    o32[:, g % OR, :].rearrange("p (s b e) -> p s b e", b=2, e=HALF),
                    slot_cols(("out", g))[:, :, 0:PW].rearrange("p s (b e) -> p s b e", b=2)[:, :, :, 0:HALF],
                    rec[:, g % NR, :].unsqueeze(2).unsqueeze(3).to_broadcast([P, G, 2, HALF]),
                    ALU.mult).then_inc(s_read["out"], 1)

            def quantise(a, coarse, fine, chain, base, s_done_):
                n_ = 0
                for dst, ks_ in ((coarse, (6, 5, 4)), (fine, (0, 1, 2, 3))):
                    for k in ks_:
                        if n_:
                            dve.wait_ge(chain, base + n_)
                        if k == ks_[0]:
                            ins = (nc.vector.tensor_scalar(dst, a, MIDS[k], 2.0, ALU.is_gt, ALU.mult) if k == 6
                                   else nc.vector.tensor_scalar(dst, a, MIDS[k], None, ALU.is_gt))
                        else:
                            ins = nc.vector.scalar_tensor_tensor(out=dst, in0=a, scalar=MIDS[k], in1=dst,
                                                                 op0=ALU.is_gt, op1=ALU.add)
                        ins.then_inc(chain, 1)
                        n_ += 1
                        yield
                dve.wait_ge(chain, base + n_)
                nc.vector.scalar_tensor_tensor(out=fine, in0=fine, scalar=0.5, in1=coarse, op0=ALU.mult,
                                               op1=ALU.add).then_inc(s_done_, 1)
                yield

            def run(gen, count):
                for _ in range(count):
                    next(gen)

            def tree(n, i):
                if i:
                    dve.wait_ge(s_tree, n * 3 + i)
                else:
                    dve.wait_ge(s_read["k"], (n + 1) * PER["k"])
                w = EC * T >> (i + 1)
                nc.vector.tensor_tensor(k_acc[:, 0:w], k_acc[:, 0:w], k_acc[:, w:2 * w], ALU.add).then_inc(s_tree, 1)

            def iteration(n):
                front, more, attend, mid, back = parts(n)
                o, m, b = n - 1, n - 2, n - 3
                first = isinstance(n, int) and n == 0
                o_first = isinstance(n, int) and n == 1
                if back:
                    dve.wait_ge(s_sig, b + 1)
                    nc.vector.tensor_tensor(sig[:, :], TB0[:, 0:FFN], sig[:, :], ALU.mult).then_inc(s_gs, 1)
                    dve.wait_ge(s_gs, b + 1)
                    dve.wait_ge(s_up, b + 1)
                    nc.vector.tensor_tensor(h[:, :], TB1[:, 0:FFN], sig[:, :], ALU.mult).then_inc(s_h, 1)
                if back:
                    dve.wait_ge(s_h, b + 1)
                    nc.vector.tensor_reduce(hsc[:, 1, :], blocks(h[:, :]), AX.X, ALU.max,
                                            apply_absolute_value=True).then_inc(s_hmax, 1)
                if front:
                    k_add(n, 1)
                if back:
                    dve.wait_ge(s_hmax, b + 1)
                    nc.vector.tensor_scalar(hsc[:, 0, :], hsc[:, 1, :], 1.0 / 6.0, 1e-12, ALU.mult,
                                            ALU.max).then_inc(s_hsc, 1)
                if front:
                    k_add(n, 2)
                if back:
                    dve.wait_ge(s_hsc, b + 1)
                    nc.vector.reciprocal(hsc[:, 1, :], hsc[:, 0, :]).then_inc(s_hrs, 1)
                if front:
                    k_add(n, 3)
                if back:
                    hquant = quantise(ha[:, :], hc[:, :], hq[:, :], s_hc, b * 7, s_hs)
                if front:
                    tree(n, 0)
                if back:
                    dve.wait_ge(s_ha, b + 1)
                    run(hquant, 1)
                if front:
                    tree(n, 1)
                if back:
                    run(hquant, 1)
                if front:
                    tree(n, 2)
                if back:
                    run(hquant, 6)

                if front:
                    dve.wait_ge(s_ks, n + 1)
                    q_scale(n, 0, first)
                if mid:
                    dve.wait_ge(s_xb, m + 1)
                    dve.wait_ge(s_y, m + 1)
                    nc.vector.tensor_tensor(r1[:, :], TB0[:, 0:DIM], x_res[:, :], ALU.add).then_inc(s_r1, 1)
                if attend:
                    norm_o(o, 0)
                if mid:
                    dve.wait_ge(s_r1, m + 1)
                    nc.vector.bn_stats(st1[:, :], r1[:, :]).then_inc(s_st1, 1)
                if attend:
                    recip(o, 0, 1)
                if mid:
                    dve.wait_ge(s_st1, m + 1)
                if attend:
                    norm_o(o, 1)
                if mid:
                    nc.vector.bn_aggr(mv1[:, :], st1[:, :]).then_inc(s_agg1, 1)
                if attend:
                    scale_o(o, 0, o_first)
                    recip(o, 1, 1)
                    scale_o(o, 1, o_first)
                if front:
                    q_scale(n, 1, first)
                if mid:
                    dve.wait_ge(s_rs1, m + 1)
                    if back:
                        dve.wait_ge(s_x1b, b + 1)
                    nc.vector.tensor_scalar(x1[:, :], r1[:, :], mv1[:, 0:1], rs1[:, 0:1], ALU.subtract,
                                            ALU.mult).then_inc(s_x1, 1)
                if attend:
                    norm_o(o, 2)
                    norm_o(o, 3)
                if mid:
                    dve.wait_ge(s_x1, m + 1)
                    nc.vector.tensor_reduce(xsc[:, 1, :], blocks(x1[:, :]), AX.X, ALU.max,
                                            apply_absolute_value=True).then_inc(s_xmax, 1)
                if attend:
                    recip(o, 2, 2)
                if mid:
                    dve.wait_ge(s_xmax, m + 1)
                    nc.vector.tensor_scalar(xsc[:, 0, :], xsc[:, 1, :], 1.0 / 6.0, 1e-12, ALU.mult,
                                            ALU.max).then_inc(s_xsc, 1)
                if attend:
                    scale_o(o, 2, o_first)
                if mid:
                    dve.wait_ge(s_xsc, m + 1)
                    nc.vector.reciprocal(xsc[:, 1, :], xsc[:, 0, :]).then_inc(s_xrs, 1)
                if attend:
                    scale_o(o, 3, o_first)
                if front:
                    q_scale(n, 2, first)
                if attend:
                    norm_o(o, 4)
                    norm_o(o, 5)
                if mid:
                    dve.wait_ge(s_xrs, m + 1)
                    dve.wait_ge(s_xabs, m + 1)
                    nc.vector.tensor_tensor(blocks(xa[:, :]), blocks(xa[:, :]), per_block(xsc[:, 1, :], x1[:, :]),
                                            ALU.mult).then_inc(s_xa, 1)
                    xquant = quantise(xa[:, :], xc[:, :], xq[:, :], s_xc, m * 7, s_xs)
                if attend:
                    recip(o, 4, 2)
                if mid:
                    dve.wait_ge(s_xa, m + 1)
                    run(xquant, 1)
                if attend:
                    scale_o(o, 4, False)
                if mid:
                    run(xquant, 1)
                if attend:
                    scale_o(o, 5, False)
                if front:
                    q_scale(n, 3, first)
                if back:
                    dve.wait_ge(s_dn, b + 1)
                    nc.vector.tensor_tensor(r2[:, :], TB0[:, 0:DIM], x1b[:, :], ALU.add).then_inc(s_r2, 1)
                if attend:
                    norm_o(o, 6)
                    norm_o(o, 7)
                if mid:
                    run(xquant, 1)
                if attend:
                    recip(o, 6, 2)
                if mid:
                    run(xquant, 1)
                if attend:
                    scale_o(o, 6, False)
                if mid:
                    run(xquant, 1)
                if attend:
                    scale_o(o, 7, False)
                if mid:
                    run(xquant, 2)
                if back:
                    dve.wait_ge(s_r2, b + 1)
                    nc.vector.bn_stats(st2[:, :], r2[:, :]).then_inc(s_st2, 1)
                if mid:
                    run(xquant, 1)

                if front:
                    v_lo(n, 0)
                if back:
                    dve.wait_ge(s_st2, b + 1)
                if more:
                    dve.wait_ge(s_xhi, n + 2)
                    nc.vector.tensor_tensor(xk[:, 1, :], TB0[:, 0:T], xk[:, 0, :], ALU.subtract).then_inc(s_xlo, 1)
                if front:
                    v_lo(n, 1)
                if back:
                    nc.vector.bn_aggr(mv2[:, :], st2[:, :]).then_inc(s_agg2, 1)
                if front:
                    v_lo(n, 2)
                    v_lo(n, 3)
                if back:
                    dve.wait_ge(s_rs2, b + 1)
                    dve.wait_ge(s_store, 16 * (b + 1))
                    nc.vector.tensor_scalar(y_out[:, :], r2[:, :], mv2[:, 0:1], rs2[:, 0:1], ALU.subtract,
                                            ALU.mult).then_inc(s_yo, 1)

            run_tiles(dve, iteration)

        @block.gpsimd
        def _(pool):
            nc.gpsimd.memset(ident[:, :], 0.0)
            nc.gpsimd.memset(both[:, :], 0.0).then_inc(s_iota, 1)
            pool.wait_ge(s_iota, 2)
            nc.gpsimd.affine_select(out=ident[:, :], in_=ident[:, :], compare_op=ALU.not_equal, fill=1.0, base=0,
                                    pattern=[[-1, P]], channel_multiplier=1)
            for i, base in enumerate((0, -DH, DH)):
                ins = nc.gpsimd.affine_select(out=both[:, :], in_=both[:, :], compare_op=ALU.not_equal, fill=1.0,
                                              base=base, pattern=[[-1, P]], channel_multiplier=1)
                if i < 2:
                    ins.then_inc(s_iota, 1)
                    pool.wait_ge(s_iota, 3 + i)
            ins.then_inc(s_const, 1)
            for k in "kv":
                pool.wait_ge(s_whi[k], 1)
                for hh in range(2):
                    hi, lo = (wmat[k][:, l].rearrange("p e (h m) -> p e h m", h=2)[:, :, hh] for l in range(2))
                    last = nc.gpsimd.tensor_tensor(lo, split_src[k][:, :, hh], hi, ALU.subtract)
                last.then_inc(s_wlo[k], 1)
            pool.wait_ge(s_wT, 1)
            nc.gpsimd.memset(vst[:, 0, :, :, HALF:VW], 1.0)
            nc.gpsimd.memset(vst[:, 1, :, :, HALF:VW], 0.0).then_inc(s_clear, 1)
            pool.wait_ge(s_whi["o"], 1)
            nc.gpsimd.tensor_tensor(w_o[:, 1, :], stage["o"], w_o[:, 0, :], ALU.subtract).then_inc(s_wlo["o"], 1)
            pool.wait_ge(s_wlo["v"], 1)
            nc.gpsimd.memset(q_bd[:, :].bitcast(F32), 0.0).then_inc(s_clear, 1)
            pool.wait_ge(s_store, 16)

            def q_lo(n, c):
                pool.wait_ge(s_qhi, n * NC + c + 1)
                e = slice(c * EC, (c + 1) * EC)
                nc.gpsimd.tensor_tensor(qnat[:, 1, :, e, :], q32[:, c % QR, :].rearrange("p (e a s) -> p a e s", a=2, s=S),
                                        qnat[:, 0, :, e, :], ALU.subtract).then_inc(s_qlo, 1)

            def o_lo(o, g):
                pool.wait_ge(s_ohi, o * NG + g + 1)
                hi, lo = (ost[:, l, :, g * G:(g + 1) * G, :].rearrange("p b s e -> p s b e") for l in range(2))
                nc.gpsimd.tensor_tensor(lo, o32[:, g % OR, :].rearrange("p (s b e) -> p s b e", b=2, e=HALF), hi,
                                        ALU.subtract).then_inc(s_olo, 1)

            def rstd(t, agg, mv, ve, rs, s_ve, s_rs):
                pool.wait_ge(agg, t + 1)
                nc.gpsimd.tensor_tensor(ve[:, :], mv[:, 1:2], consts[:, 1:2], ALU.add).then_inc(s_ve, 1)
                pool.wait_ge(s_ve, t + 1)
                nc.gpsimd.tensor_tensor(rs[:, :], ve[:, :], consts[:, 0:1], ALU.pow).then_inc(s_rs, 1)

            def iteration(n):
                front, more, attend, mid, back = parts(n)
                o, m, b = n - 1, n - 2, n - 3
                if back:
                    pool.wait_ge(s_hrs, b + 1)
                    pool.wait_ge(s_habs, b + 1)
                    nc.gpsimd.tensor_tensor(blocks(ha[:, :]), blocks(ha[:, :]), per_block(hsc[:, 1, :], h[:, :]),
                                            ALU.mult).then_inc(s_ha, 1)
                    pool.wait_ge(s_hsgn, b + 1)
                    pool.wait_ge(s_hsc, b + 1)
                    nc.gpsimd.tensor_tensor(blocks(hss[:, :]), blocks(hsgn[:, :]), per_block(hsc[:, 0, :], h[:, :]),
                                            ALU.mult).then_inc(s_hss, 1)
                if back:
                    nc.gpsimd.tensor_copy(x1b[:, :], x1[:, :]).then_inc(s_x1b, 1)
                if mid:
                    pool.wait_ge(s_xres, (m + 1) * 16)
                    nc.gpsimd.tensor_tensor(x_res[:, :], x_res[:, :], bo_b[:, :], ALU.add).then_inc(s_xb, 1)
                if back:
                    pool.wait_ge(s_hss, b + 1)
                    pool.wait_ge(s_hs, b + 1)
                    nc.gpsimd.tensor_tensor(hq[:, :], hq[:, :], hss[:, :], ALU.mult).then_inc(s_hq, 1)
                if mid:
                    rstd(m, s_agg1, mv1, ve1, rs1, s_ve1, s_rs1)
                for g in range(NG):
                    if mid and g == NG - 1:
                        pool.wait_ge(s_xss, m + 1)
                        pool.wait_ge(s_xs, m + 1)
                        nc.gpsimd.tensor_tensor(xq[:, :], xq[:, :], xsgn[:, :], ALU.mult).then_inc(s_xq, 1)
                    if attend:
                        o_lo(o, g)
                    if mid and g == 4:
                        pool.wait_ge(s_xsgn, m + 1)
                        pool.wait_ge(s_xsc, m + 1)
                        nc.gpsimd.tensor_tensor(blocks(xsgn[:, :]), blocks(xsgn[:, :]), per_block(xsc[:, 0, :], x1[:, :]),
                                                ALU.mult).then_inc(s_xss, 1)
                if front:
                    q_lo(n, 0)
                if back:
                    rstd(b, s_agg2, mv2, ve2, rs2, s_ve2, s_rs2)
                if front:
                    q_lo(n, 1)
                    q_lo(n, 2)
                    q_lo(n, 3)

            run_tiles(pool, iteration)


_INS = ['L0_attn_x', 'L0_attn_Wq', 'L0_attn_Wk', 'L0_attn_Wv', 'L0_attn_Wo', 'L0_attn_bo', 'L0_ffn_w_gate',
        'L0_ffn_w_up', 'L0_ffn_w_down']


def kernel(**inputs):
    import numpy as _np
    import concourse.bacc as _bacc
    from concourse import mybir as _mybir
    from concourse.bass_utils import run_bass_kernel_spmd as _run

    nc = _bacc.Bacc("TRN2", target_bir_lowering=False, num_devices=1)
    arrays, args = {}, []
    for name in _INS:
        a = _np.ascontiguousarray(inputs[name])
        arrays[f"in_{name}"] = a
        args.append(nc.dram_tensor(f"in_{name}", a.shape, _mybir.dt.from_np(a.dtype), kind="ExternalInput").ap())
    shape = inputs['L0_attn_x'].shape
    args.append(nc.dram_tensor("out_0", tuple(shape), _mybir.dt.float32, kind="ExternalOutput").ap())
    attention_ffn(nc, *args)
    r = _run(nc, [arrays], core_ids=[0])
    return r.results[0]["out_0"]
```
